# Optimizing a Trainium2 kernel written in Bass

```python
import numpy as np
import jax
import jax.numpy as jnp

def _softmax(x, axis=-1):
    return jax.nn.softmax(x, axis=axis)

def _gelu(x):
    return jax.nn.gelu(x, approximate=True)

def _silu(x):
    return jax.nn.silu(x)

def _sigmoid(x):
    return jax.nn.sigmoid(x)

def _layernorm(x, axis=-1, eps=1e-05):
    m = jnp.mean(x, axis=axis, keepdims=True)
    v = jnp.var(x, axis=axis, keepdims=True)
    return (x - m) / jnp.sqrt(v + eps)

def _scatter_add(tgt, idx, src, axis=0):
    return tgt.at[idx].add(src)

def _segment_sum(src, seg, n):
    return jax.ops.segment_sum(src, seg, n)
kernel_name = 'mk_gnn_preln_d2_gnn_r32_00412c'

def setup_inputs(seed: int=0):
    np.random.seed(seed)
    _w = jnp.asarray

    def _rec_inputs():
        import jax
        import jax.numpy as jnp
        _gk = jax.random.key(seed)
        x = -0.000202 + 1 * jax.random.normal(jax.random.fold_in(_gk, 1), (3125, 128), jnp.float32)
        src = jax.random.randint(jax.random.fold_in(_gk, 2), (50000,), 0, 3125, jnp.int32)
        dst = jax.random.randint(jax.random.fold_in(_gk, 3), (50000,), 0, 3125, jnp.int32)
        _o = jnp.argsort(dst, stable=True)
        src = src[_o]
        dst = dst[_o]
        return (x, src, dst)
    x, src, dst = _rec_inputs()

    def _L0_gnn_setup():
        import jax, jax.numpy as jnp
        import numpy as np
        N_NODES = 50000
        N_EDGES = 25000
        D_IN, D_HID, D_OUT = (128, 256, 128)
        key = jax.random.key(seed)
        ks = jax.random.split(key, 12)
        inp = {'x': jax.random.normal(ks[0], (N_NODES, D_IN), dtype=jnp.float32), 'edge_src': jax.random.randint(ks[1], (N_EDGES,), 0, N_NODES, dtype=jnp.int32), 'edge_dst': jax.random.randint(ks[2], (N_EDGES,), 0, N_NODES, dtype=jnp.int32)}

        def lin(k, fi, fo):
            return jax.random.normal(k, (fi, fo), dtype=jnp.float32) * (1.0 / np.sqrt(fi))
        inp['Ws0'] = lin(ks[3], D_IN, D_HID)
        inp['Wn0'] = lin(ks[4], D_IN, D_HID)
        inp['b0'] = jnp.zeros((D_HID,), jnp.float32)
        inp['Ws1'] = lin(ks[5], D_HID, D_HID)
        inp['Wn1'] = lin(ks[6], D_HID, D_HID)
        inp['b1'] = jnp.zeros((D_HID,), jnp.float32)
        inp['Ws2'] = lin(ks[7], D_HID, D_OUT)
        inp['Wn2'] = lin(ks[8], D_HID, D_OUT)
        inp['b2'] = jnp.zeros((D_OUT,), jnp.float32)
        return inp
    _L0_gnn_all = _L0_gnn_setup()
    _L0_gnn_in = {k: v for k, v in _L0_gnn_all.items() if k in ('Ws0', 'Wn0', 'b0', 'Ws1', 'Wn1', 'b1', 'Ws2', 'Wn2', 'b2')}
    del _L0_gnn_all

    def _L1_gnn_setup():
        import jax, jax.numpy as jnp
        import numpy as np
        N = 50000
        E = 25000
        D = 128
        H = 8
        DH = D // H
        L = 2
        LN_EPS = 1e-05

        def layer_norm(x, w, b):
            m = jnp.mean(x, axis=-1, keepdims=True)
            v = jnp.mean((x - m) ** 2, axis=-1, keepdims=True)
            return (x - m) * jax.lax.rsqrt(v + LN_EPS) * w + b
        key = jax.random.key(seed)
        ks = jax.random.split(key, 16)
        s = 0.05

        def nrm(k, shape):
            return jax.random.normal(k, shape, jnp.float32) * s
        inp = {'h': jax.random.normal(ks[0], (N, D), jnp.float32), 'src': jax.random.randint(ks[1], (E,), 0, N), 'dst': jax.random.randint(ks[2], (E,), 0, N), 'W_emb': nrm(ks[3], (D, D)), 'Wq': nrm(ks[4], (L, D, D)), 'bq': jnp.zeros((L, D), jnp.float32), 'Wk': nrm(ks[5], (L, D, D)), 'bk': jnp.zeros((L, D), jnp.float32), 'Wv': nrm(ks[6], (L, D, D)), 'bv': jnp.zeros((L, D), jnp.float32), 'Wo': nrm(ks[7], (L, D, D)), 'bo': jnp.zeros((L, D), jnp.float32), 'ln1_w': jnp.ones((L, D), jnp.float32), 'ln1_b': jnp.zeros((L, D), jnp.float32), 'Wf1': nrm(ks[8], (L, D, 2 * D)), 'bf1': jnp.zeros((L, 2 * D), jnp.float32), 'Wf2': nrm(ks[9], (L, 2 * D, D)), 'bf2': jnp.zeros((L, D), jnp.float32), 'ln2_w': jnp.ones((L, D), jnp.float32), 'ln2_b': jnp.zeros((L, D), jnp.float32)}
        return inp
    _L1_gnn_all = _L1_gnn_setup()
    _L1_gnn_in = {k: v for k, v in _L1_gnn_all.items() if k in ('W_emb', 'Wq', 'bq', 'Wk', 'bk', 'Wv', 'bv', 'Wo', 'bo', 'ln1_w', 'ln1_b', 'Wf1', 'bf1', 'Wf2', 'bf2', 'ln2_w', 'ln2_b')}
    del _L1_gnn_all
    return {'x': x, 'src': src, 'dst': dst, 'L0_gnn_Ws0': _L0_gnn_in['Ws0'], 'L0_gnn_Wn0': _L0_gnn_in['Wn0'], 'L0_gnn_b0': _L0_gnn_in['b0'], 'L0_gnn_Ws1': _L0_gnn_in['Ws1'], 'L0_gnn_Wn1': _L0_gnn_in['Wn1'], 'L0_gnn_b1': _L0_gnn_in['b1'], 'L0_gnn_Ws2': _L0_gnn_in['Ws2'], 'L0_gnn_Wn2': _L0_gnn_in['Wn2'], 'L0_gnn_b2': _L0_gnn_in['b2'], 'L1_gnn_W_emb': _L1_gnn_in['W_emb'], 'L1_gnn_Wq': _L1_gnn_in['Wq'], 'L1_gnn_bq': _L1_gnn_in['bq'], 'L1_gnn_Wk': _L1_gnn_in['Wk'], 'L1_gnn_bk': _L1_gnn_in['bk'], 'L1_gnn_Wv': _L1_gnn_in['Wv'], 'L1_gnn_bv': _L1_gnn_in['bv'], 'L1_gnn_Wo': _L1_gnn_in['Wo'], 'L1_gnn_bo': _L1_gnn_in['bo'], 'L1_gnn_ln1_w': _L1_gnn_in['ln1_w'], 'L1_gnn_ln1_b': _L1_gnn_in['ln1_b'], 'L1_gnn_Wf1': _L1_gnn_in['Wf1'], 'L1_gnn_bf1': _L1_gnn_in['bf1'], 'L1_gnn_Wf2': _L1_gnn_in['Wf2'], 'L1_gnn_bf2': _L1_gnn_in['bf2'], 'L1_gnn_ln2_w': _L1_gnn_in['ln2_w'], 'L1_gnn_ln2_b': _L1_gnn_in['ln2_b']}

def reference(x, src, dst, L0_gnn_Ws0, L0_gnn_Wn0, L0_gnn_b0, L0_gnn_Ws1, L0_gnn_Wn1, L0_gnn_b1, L0_gnn_Ws2, L0_gnn_Wn2, L0_gnn_b2, L1_gnn_W_emb, L1_gnn_Wq, L1_gnn_bq, L1_gnn_Wk, L1_gnn_bk, L1_gnn_Wv, L1_gnn_bv, L1_gnn_Wo, L1_gnn_bo, L1_gnn_ln1_w, L1_gnn_ln1_b, L1_gnn_Wf1, L1_gnn_bf1, L1_gnn_Wf2, L1_gnn_bf2, L1_gnn_ln2_w, L1_gnn_ln2_b):
    import jax
    import jax.numpy as jnp

    def _L0_gnn_ref(x, edge_src, edge_dst, Ws0, Wn0, b0, Ws1, Wn1, b1, Ws2, Wn2, b2):
        import jax, jax.numpy as jnp
        import numpy as np
        N_NODES = 50000
        N_EDGES = 25000
        D_IN, D_HID, D_OUT = (128, 256, 128)
        n = x.shape[0]
        deg = jax.ops.segment_sum(jnp.ones(edge_dst.shape, x.dtype), edge_dst, num_segments=n)
        inv_deg = jnp.where(deg > 0, 1.0 / jnp.maximum(deg, 1.0), 0.0)[:, None]

        def sage_conv(h, Ws, Wn, b):
            agg = jax.ops.segment_sum(h[edge_src], edge_dst, num_segments=n)
            h_neigh = agg * inv_deg
            return h @ Ws + h_neigh @ Wn + b
        h = jax.nn.relu(sage_conv(x, Ws0, Wn0, b0))
        h = jax.nn.relu(sage_conv(h, Ws1, Wn1, b1))
        h = jax.nn.relu(sage_conv(h, Ws2, Wn2, b2))
        return h

    def _L1_gnn_ref(h, src, dst, W_emb, Wq, bq, Wk, bk, Wv, bv, Wo, bo, ln1_w, ln1_b, Wf1, bf1, Wf2, bf2, ln2_w, ln2_b):
        import jax, jax.numpy as jnp
        import numpy as np
        N = 50000
        E = 25000
        D = 128
        H = 8
        DH = D // H
        L = 2
        LN_EPS = 1e-05

        def layer_norm(x, w, b):
            m = jnp.mean(x, axis=-1, keepdims=True)
            v = jnp.mean((x - m) ** 2, axis=-1, keepdims=True)
            return (x - m) * jax.lax.rsqrt(v + LN_EPS) * w + b
        n = h.shape[0]
        scale = 1.0 / np.sqrt(DH)
        h = h @ W_emb
        for l in range(L):
            q = (h @ Wq[l] + bq[l]).reshape(n, H, DH)
            k = (h @ Wk[l] + bk[l]).reshape(n, H, DH)
            v = (h @ Wv[l] + bv[l]).reshape(n, H, DH)
            s = jnp.einsum('ehd,ehd->eh', k[src], q[dst]) * scale
            s = jnp.exp(jnp.clip(s, -5.0, 5.0))
            wV = jax.ops.segment_sum(v[src] * s[:, :, None], dst, num_segments=n)
            z = jax.ops.segment_sum(s, dst, num_segments=n)
            attn = (wV / (z[:, :, None] + 1e-06)).reshape(n, D)
            hx = layer_norm(h + attn @ Wo[l] + bo[l], ln1_w[l], ln1_b[l])
            ffn = jax.nn.relu(hx @ Wf1[l] + bf1[l]) @ Wf2[l] + bf2[l]
            h = layer_norm(hx + ffn, ln2_w[l], ln2_b[l])
        return h
    h = jnp.maximum(_layernorm(x, axis=-1), 0.0)
    x = x + _L0_gnn_ref(h, src, dst, L0_gnn_Ws0, L0_gnn_Wn0, L0_gnn_b0, L0_gnn_Ws1, L0_gnn_Wn1, L0_gnn_b1, L0_gnn_Ws2, L0_gnn_Wn2, L0_gnn_b2)
    h = jnp.maximum(_layernorm(x, axis=-1), 0.0)
    x = x + _L1_gnn_ref(h, src, dst, L1_gnn_W_emb, L1_gnn_Wq, L1_gnn_bq, L1_gnn_Wk, L1_gnn_bk, L1_gnn_Wv, L1_gnn_bv, L1_gnn_Wo, L1_gnn_bo, L1_gnn_ln1_w, L1_gnn_ln1_b, L1_gnn_Wf1, L1_gnn_bf1, L1_gnn_Wf2, L1_gnn_bf2, L1_gnn_ln2_w, L1_gnn_ln2_b)
    return x

_drawn_inputs = setup_inputs


def setup_inputs(seed=0):
    import zlib

    import numpy as np

    out = dict(_drawn_inputs(seed))
    spreads = {'L0_gnn_b0': (0.0, 0.1),
     'L0_gnn_b1': (0.0, 0.1),
     'L0_gnn_b2': (0.0, 0.1),
     'L1_gnn_bq': (0.0, 0.8),
     'L1_gnn_bk': (0.0, 0.8),
     'L1_gnn_bv': (0.0, 0.1),
     'L1_gnn_bo': (0.0, 0.1),
     'L1_gnn_ln1_w': (1.0, 0.2),
     'L1_gnn_ln1_b': (0.0, 0.1),
     'L1_gnn_bf1': (0.0, 0.1),
     'L1_gnn_bf2': (0.0, 0.1),
     'L1_gnn_ln2_w': (1.0, 0.2),
     'L1_gnn_ln2_b': (0.0, 0.1)}
    factors = {'L1_gnn_Wq': 5.936, 'L1_gnn_Wk': 5.595}
    for name, (base, spread) in spreads.items():
        noise = np.random.default_rng([zlib.crc32(name.encode()), seed]).standard_normal(out[name].shape)
        drawn = base * np.exp(spread * noise) if base else spread * noise
        out[name] = jnp.asarray(drawn.astype(out[name].dtype))
    for name, factor in factors.items():
        out[name] = (out[name] * factor).astype(out[name].dtype)
    return out
```

```python
import concourse.bass as bass
from concourse import mybir
from contextlib import ExitStack


def gnn_kernel(nc, x, src, dst, Ws0, Wn0, b0, Ws1, Wn1, b1, Ws2, Wn2, b2, W_emb, Wq, bq, Wk, bk, Wv, bv,
               Wo, bo, ln1_w, ln1_b, Wf1, bf1, Wf2, bf2, ln2_w, ln2_b, out):
    fp32 = mybir.dt.float32
    i32 = mybir.dt.int32
    ALU = mybir.AluOpType
    ACT = mybir.ActivationFunctionType
    AX = mybir.AxisListType.X
    DVE, PE = mybir.EngineType.DVE, mybir.EngineType.PE
    ds = bass.ds

    NODES, D = x.shape
    EDGES = src.shape[0]
    HID = Ws0.shape[1]
    LAYERS = Wq.shape[0]
    HEADS = 8
    DH = D // HEADS
    P = 128
    NT = 125
    TILES = NODES // NT
    GROUP = 5
    GROUPS = TILES // GROUP
    ETILES = -(-EDGES // P)
    CH = -(-ETILES // P)
    HALF = 8
    RING = 2 * HALF
    STEPS = -(-(ETILES + TILES - 1) // RING) * RING
    ITERS = STEPS // RING
    HALVES = STEPS // HALF
    WMAX = HID + 1
    MW = D + HEADS
    PAD_DST = 1000000
    EPS = 1e-5
    Z_EPS = 1e-6
    SPLIT = NT // 16 * 16

    rows_w = nc.dram_tensor("rows_w", [NODES, HID], fp32, kind="Internal").ap()
    rows_n = nc.dram_tensor("rows_n", [NODES, D], fp32, kind="Internal").ap()
    rows_w_t = rows_w.rearrange("(t p) w -> p t w", p=NT)
    rows_n_t = rows_n.rearrange("(t p) w -> p t w", p=NT)
    x_t = x.rearrange("(t p) w -> p t w", p=NT)
    out_t = out.rearrange("(t p) w -> p t w", p=NT)

    with ExitStack() as ctx:
        def sb(name, shape, dt=fp32):
            return ctx.enter_context(nc.sbuf_tensor(name, shape, dt))

        def sem(name):
            return ctx.enter_context(nc.semaphore(name))

        iota_int = sb("iota_int", [P, STEPS], i32)
        thr_int = sb("thr_int", [P, TILES - 1], i32)
        tcol_int = sb("tcol_int", [P, CH], i32)
        iota_f = sb("iota_f", [P, STEPS])
        thr = sb("thr", [P, TILES - 1])
        tcol = sb("tcol", [P, CH])
        ident = sb("ident", [P, P])
        step_src = sb("step_src", [P, STEPS], i32)
        step_dst = sb("step_dst", [P, STEPS + HALF])
        step_tile = sb("step_tile", [P, STEPS], i32)
        idx_ring = sb("idx_ring", [P, 2, HALF], i32)
        xs = sb("xs", [NT, TILES, D])
        S = sb("S", [NT, TILES, HID])
        h = S[:, :, 0:D]
        hx = S[:, :, D:2 * D]
        acc = sb("acc", [P, TILES, WMAX])
        y = sb("y", [NT, TILES, D])
        q = sb("q", [NT, TILES, D])
        G = sb("G", [NT, 2, GROUP, HID])
        hT = sb("hT", [P, 2, TILES, NT])
        inv_deg = sb("inv_deg", [NT, TILES])
        col_a = sb("col_a", [NT, TILES])
        col_b = sb("col_b", [NT, TILES])
        zr = sb("zr", [NT, TILES, HEADS])
        W0 = sb("W0", [P, 2, HID])
        W1 = sb("W1", [P, 2, 2, HID])
        W2 = sb("W2", [P, 2, 2, D])
        We = sb("We", [P, D])
        Wqkv = sb("Wqkv", [P, 3, D])
        Wo_s = sb("Wo_s", [P, D])
        Wf1_s = sb("Wf1_s", [P, 2 * D])
        Wf2_s = sb("Wf2_s", [P, 2, D])
        bias_s = sb("bias_s", [NT, 2, HID])
        bias_n = sb("bias_n", [NT, D])
        brow = sb("brow", [NT, LAYERS, 9, D])
        bf1_col = sb("bf1_col", [P, LAYERS, 2])
        slots = sb("slots", [P, RING, WMAX])
        onehot = sb("onehot", [P, 2, HALF, NT])
        onehotT = sb("onehotT", [NT, HALF, P])
        prod = sb("prod", [P, HALF, D])
        score = sb("score", [P, HALF, HEADS])
        clipped = sb("clipped", [P, HALF, HEADS])
        msg = sb("msg", [P, 2, HALF, MW])
        raw = y[:, :, :]
        edge_i = sb("edge_i", [P, 2, CH, P], i32)
        edge_f = slots[:, 0:8, 0:P]
        hit = hT[:, 0, :, :].rearrange("p t n -> p (t n)")[:, 0:CH * STEPS].rearrange("p (c s) -> p c s", c=CH)
        step_edge = hT[:, 1, :, :].rearrange("p t n -> p (t n)")[:, 0:STEPS]
        step_base = hT[:, 1, :, :].rearrange("p t n -> p (t n)")[:, STEPS:2 * STEPS]
        ge = sb("ge", [P, CH, TILES - 1])
        key = sb("key", [P, CH])
        live = sb("live", [P, CH])
        ones = sb("ones", [P, P])
        fT = acc[:, :, :].rearrange("p t w -> p (t w)")[:, 0:2 * TILES * NT].rearrange(
            "p (k t n) -> p k t n", k=2, t=TILES)

        ps = ctx.enter_context(nc.psum_tensor("ps", [P, 8, 512], fp32))
        flat = ps[:, :, :].rearrange("p b n -> p (b n)")
        psT = flat[:, 0:GROUP * P].rearrange("p (j n) -> p j n", j=GROUP)

        def psM(n, w):
            o = 1024 + 1536 * (n % 2)
            return flat[0:NT, o:o + GROUP * w].rearrange("p (j n) -> p j n", j=GROUP)

        psOT = flat[0:NT, 0:HALF * P].rearrange("p (j n) -> p j n", j=HALF)
        psQ = flat[:, 1024:1024 + HALF * D].rearrange("p (j n) -> p j n", j=HALF)

        def psA(j):
            return ps[0:NT, 4 + j % 4, 0:MW]

        iota_ready = sem("iota_ready")
        edges_padded = sem("edges_padded")
        edges_loaded = sem("edges_loaded")
        x_loaded = sem("x_loaded")
        w_loaded = sem("w_loaded")
        bias_loaded = sem("bias_loaded")
        layer_w_loaded = sem("layer_w_loaded")
        layer_w_used = sem("layer_w_used")
        hits_ready = sem("hits_ready")
        counts_ready = sem("counts_ready")
        picks_ready = sem("picks_ready")
        rows_picked = sem("rows_picked")
        table_ready = sem("table_ready")
        dve_order = sem("dve_order")
        nodes_ready = sem("nodes_ready")
        var_ready = sem("var_ready")
        std_ready = sem("std_ready")
        t_done = sem("t_done")
        t_evac = sem("t_evac")
        m_done = sem("m_done")
        m_evac = sem("m_evac")
        f_done = sem("f_done")
        f_evac = sem("f_evac")
        rows_stored = [sem("rows_stored_a"), sem("rows_stored_b")]
        steps_go = sem("steps_go")
        pool_step = sem("pool_step")
        idx_copied = sem("idx_copied")
        gathered = [sem(f"gathered{b}") for b in range(RING)]
        half_free = sem("half_free")
        onehot_ready = sem("onehot_ready")
        onehot_free = sem("onehot_free")
        summed = sem("summed")
        added = sem("added")
        oT_done = sem("oT_done")
        oT_evac = sem("oT_evac")
        q_done = sem("q_done")
        prod_done = sem("prod_done")
        score_done = sem("score_done")
        clip_done = sem("clip_done")
        exp_done = sem("exp_done")
        msg_ready = sem("msg_ready")
        out_ready = sem("out_ready")
        out_stored = sem("out_stored")

        block = ctx.enter_context(nc.Block())

        ROW_STAGES = [(0, HID), (1, HID), (2, D)] + [(3 + l, 2 * D) for l in range(LAYERS)]
        STAGE = {}
        for name in ["n0", "s0", "n1", "s1", "n2", "s2", "emb"] + [
                f"{s}{l}" for l in range(LAYERS) for s in ("kv", "q", "o", "f")]:
            STAGE[name] = len(STAGE)
        TSTAGE = {}
        for name in ["t0", "t1a", "t1b", "t2a", "t2b", "te"] + [
                f"{s}{l}" for l in range(LAYERS) for s in ("th", "ta", "tx")]:
            TSTAGE[name] = len(TSTAGE)
        NODES_READY = {n: k + 1 for k, n in enumerate(
            ["t0", "t1", "t2", "te"] + [f"{s}{l}" for l in range(LAYERS) for s in ("th", "ta", "tx")])}
        LN = {n: k + 1 for k, n in enumerate(
            ["ln0", "lne"] + [f"{s}{l}" for l in range(LAYERS) for s in ("ln1_", "ln2_")])}

        @block.sync
        def _(sp):
            sp.wait_ge(edges_padded, 2)
            full = EDGES // P
            for n, a in enumerate((dst, src)):
                whole = (CH - 1) * P
                sp.dma_start(edge_i[:, n, 0:CH - 1, :],
                             a[0:whole * P].rearrange("(c p e) -> p c e", p=P, e=P)).then_inc(edges_loaded, 16)
                sp.dma_start(edge_i[0:full - whole, n, CH - 1, :],
                             a[whole * P:full * P].rearrange("(p e) -> p e", e=P)).then_inc(edges_loaded, 16)
                sp.dma_start(edge_i[full - whole:full - whole + 1, n, CH - 1, 0:EDGES - full * P],
                             a[full * P:EDGES].rearrange("(p e) -> p e", p=1)).then_inc(edges_loaded, 16)
            sp.dma_start(xs[0:SPLIT, :, :], x_t[0:SPLIT]).then_inc(x_loaded, 16)
            sp.dma_start(xs[SPLIT:NT, :, :], x_t[SPLIT:NT]).then_inc(x_loaded, 16)

            def store_rows(stage):
                s, w = ROW_STAGES[stage]
                name = ["n0", "n1", "n2"][s] if s < 3 else f"kv{s - 3}"
                dram = rows_n_t if w == D else rows_w_t
                for g in range(GROUPS):
                    sp.wait_ge(m_evac, STAGE[name] * GROUPS + g + 1 + 2)
                    for lo, hi in ((0, SPLIT), (SPLIT, NT)):
                        sp.dma_start(dram[lo:hi, g * GROUP:(g + 1) * GROUP, :],
                                     G[lo:hi, g % 2, :, 0:w]).then_inc(rows_stored[g % 2], 16)

            for s in range(3):
                store_rows(s)
            for l in range(LAYERS):
                store_rows(3 + l)
            sp.wait_ge(out_ready, 1)
            sp.dma_start(out_t[0:SPLIT], y[0:SPLIT, :, :]).then_inc(out_stored, 16)
            sp.dma_start(out_t[SPLIT:NT], y[SPLIT:NT, :, :]).then_inc(out_stored, 16)
            sp.wait_ge(out_stored, 32)

        def stored(s, g):
            per = [sum(1 for k in range(GROUPS) if k % 2 == b) for b in range(2)]
            return (s * per[g % 2] + g // 2 + 1) * 32

        @block.gpsimd
        def _(pool):
            pool.iota(iota_int[:, :], pattern=[[1, STEPS]], base=0, channel_multiplier=0).then_inc(iota_ready, 1)
            pool.iota(thr_int[:, :], pattern=[[NT, TILES - 1]], base=NT, channel_multiplier=0).then_inc(iota_ready, 1)
            pool.iota(tcol_int[:, :], pattern=[[P, CH]], base=0, channel_multiplier=1).then_inc(iota_ready, 1)
            pool.wait_ge(table_ready, 1)
            for s in range(len(ROW_STAGES)):
                w = ROW_STAGES[s][1]
                rows = rows_n if w == D else rows_w
                pool.wait_ge(rows_stored[0], stored(s, GROUPS - 1 - (GROUPS - 1) % 2))
                pool.wait_ge(rows_stored[1], stored(s, GROUPS - 1 - GROUPS % 2))
                with pool.Fori(0, ITERS) as it:
                    for half in range(2):
                        pool.wait_ge(half_free, s * HALVES + it * 2 + half + 1)
                        pool.sem_inc(pool_step, 1)
                        pool.tensor_copy(idx_ring[:, half, :],
                                         step_src[:, ds(it * RING + half * HALF, HALF)]).then_inc(idx_copied, 1)
                        pool.wait_ge(idx_copied, s * HALVES + it * 2 + half + 1)
                        pool.sem_inc(pool_step, 1)
                        for j in range(HALF):
                            b = half * HALF + j
                            pool.indirect_dma_start(
                                out=slots[:, b, 0:w], out_offset=None, in_=rows,
                                in_offset=bass.IndirectOffsetOnAxis(ap=idx_ring[:, half, j:j + 1], axis=0),
                            ).then_inc(gathered[b], 16)

        @block.scalar
        def _(act):
            loads = [
                (W0[:, 0, :], Wn0), (W0[:, 1, :], Ws0),
                (W1[:, 0, :, :], Wn1.rearrange("(k p) n -> p k n", p=P)),
                (W1[:, 1, :, :], Ws1.rearrange("(k p) n -> p k n", p=P)),
                (W2[:, 0, :, :], Wn2.rearrange("(k p) n -> p k n", p=P)),
                (W2[:, 1, :, :], Ws2.rearrange("(k p) n -> p k n", p=P)),
                (We[:, :], W_emb),
            ]
            for a, b in loads:
                act.dma_start(a, b).then_inc(w_loaded, 16)

            def row(v):
                return v.rearrange("(a n) -> a n", a=1).to_broadcast([NT, v.shape[0]])
            vectors = [(bias_s[:, 0, :], row(b0)), (bias_s[:, 1, :], row(b1)), (bias_n[:, :], row(b2))]
            for l in range(LAYERS):
                for k, v in enumerate((bk, bv, bq, bo, bf2, ln1_w, ln1_b, ln2_w, ln2_b)):
                    vectors.append((brow[:, l, k, :], row(v[l])))
                for c in range(2):
                    vectors.append((bf1_col[:, l, c:c + 1],
                                    bf1[l, c * P:(c + 1) * P].rearrange("(p a) -> p a", a=1)))
            for a, b in vectors:
                act.dma_start(a, b).then_inc(bias_loaded, 16)

            def load_layer(l):
                if l > 0:
                    act.wait_ge(layer_w_used, l)
                for a, b in ((Wqkv[:, 0, :], Wk[l]), (Wqkv[:, 1, :], Wv[l]), (Wqkv[:, 2, :], Wq[l]),
                             (Wo_s[:, :], Wo[l]), (Wf1_s[:, :], Wf1[l]),
                             (Wf2_s[:, :, :], Wf2[l].rearrange("(k p) n -> p k n", p=P))):
                    act.dma_start(a, b).then_inc(layer_w_loaded, 16)

            load_layer(0)

            def evac_t(name, k, func):
                for g in range(GROUPS):
                    n = TSTAGE[name] * GROUPS + g
                    act.wait_ge(t_done, n + 1)
                    act.activation(hT[:, k, g * GROUP:(g + 1) * GROUP, :], psT[:, :, 0:NT], func).then_inc(t_evac, 1)

            def std(name):
                act.wait_ge(var_ready, LN[name])
                act.activation(col_b[:, :], col_a[:, :], ACT.Sqrt).then_inc(std_ready, 1)

            std("ln0")
            evac_t("t0", 0, ACT.Relu)
            evac_t("t1a", 0, ACT.Relu)
            evac_t("t1b", 1, ACT.Relu)
            evac_t("t2a", 0, ACT.Relu)
            evac_t("t2b", 1, ACT.Relu)
            std("lne")
            evac_t("te", 0, ACT.Relu)
            for l in range(LAYERS):
                evac_t(f"th{l}", 0, ACT.Copy)

                def evac_onehot(n):
                    act.wait_ge(oT_done, n + 1)
                    act.activation(onehotT[:, :, :], psOT, ACT.Copy).then_inc(oT_evac, 1)

                evac_onehot(l * (HALVES + 1))
                with act.Fori(0, ITERS) as it:
                    for half in range(2):
                        n = l * HALVES + it * 2 + half
                        act.wait_ge(oT_done, n + l + 2)
                        act.wait_ge(q_done, n + 1)
                        act.activation(onehotT[:, :, :], psOT, ACT.Copy).then_inc(oT_evac, 1)
                        act.wait_ge(clip_done, n + 1)
                        act.wait_ge(onehot_free, 3 * HALVES + n + 1)
                        act.activation(msg[:, half, :, D:MW], clipped[:, :, :], ACT.Exp).then_inc(exp_done, 1)

                evac_t(f"ta{l}", 0, ACT.Copy)
                std(f"ln1_{l}")
                evac_t(f"tx{l}", 0, ACT.Copy)
                for c in range(2):
                    for g in range(GROUPS):
                        n = (l * 2 + c) * GROUPS + g
                        act.wait_ge(f_done, n + 1)
                        act.activation(fT[:, c, g * GROUP:(g + 1) * GROUP, :], psT[:, :, 0:NT], ACT.Relu,
                                       bias=bf1_col[:, l, c:c + 1]).then_inc(f_evac, 1)
                if l + 1 < LAYERS:
                    load_layer(l + 1)
                std(f"ln2_{l}")

        @block.tensor
        def _(pe):
            pe.sem_inc(half_free, 2)
            pe.sem_inc(onehot_free, 2)
            pe.sem_inc(added, 2)
            pe.sem_inc(m_evac, 2)
            pe.wait_ge(hits_ready, 1)
            for c in range(CH):
                last = pe.matmul(ps[:, 0, 0:STEPS], ones[:, :], hit[:, c, :], start=c == 0, stop=c == CH - 1)
            last.then_inc(counts_ready, 1)
            pe.wait_ge(picks_ready, 1)
            for n in range(2):
                for c in range(CH):
                    last = pe.matmul(ps[:, 1 + n, 0:STEPS], edge_f[:, n * CH + c, :], hit[:, c, :],
                                     start=c == 0, stop=c == CH - 1)
                last.then_inc(rows_picked, 1)
            pe.wait_ge(table_ready, 1)

            def transposes(name, src_tile, ready):
                for g in range(GROUPS):
                    n = TSTAGE[name] * GROUPS + g
                    pe.wait_ge(nodes_ready, ready)
                    if n > 0:
                        pe.wait_ge(t_evac, n)
                    for j in range(GROUP):
                        last = pe.transpose(psT[:, j, 0:NT], src_tile(g * GROUP + j), ident[0:NT, 0:NT])
                    last.then_inc(t_done, 1)

            def products(name, w, kk, operand, weight, need=None):
                for g in range(GROUPS):
                    n = STAGE[name] * GROUPS + g
                    pe.wait_ge(m_evac, n + 1)
                    if need:
                        pe.wait_ge(need[0], need[1] + g)
                    for j in range(GROUP):
                        for k in range(kk):
                            last = pe.matmul(psM(n, w)[:, j, :], operand(k, g * GROUP + j), weight(k),
                                             start=k == 0, stop=k == kk - 1)
                    last.then_inc(m_done, 1)

            def hT_tile(k, t):
                return hT[:, k, t, :]

            def t_ready(name):
                return (t_evac, TSTAGE[name] * GROUPS + 1)

            def sage_steps(s, w):
                with pe.Fori(0, ITERS) as it:
                    for half in range(2):
                        pe.wait_ge(onehot_ready, s * HALVES + it * 2 + half + 1)
                        for j in range(HALF):
                            n = s * STEPS + it * RING + half * HALF + j
                            b = half * HALF + j
                            pe.wait_ge(added, n + 1)
                            pe.wait_ge(gathered[b], (s * ITERS + it + 1) * 16)
                            last = pe.matmul(ps[0:NT, 2 + j % 2, 0:w], onehot[:, half, j, :], slots[:, b, 0:w],
                                             start=True, stop=True)
                            last.then_inc(summed, 1)
                        pe.wait_ge(summed, s * STEPS + it * RING + half * HALF + HALF)
                        pe.sem_inc(half_free, 1)
                        pe.sem_inc(onehot_free, 1)

            pe.wait_ge(w_loaded, 7 * 16)
            transposes("t0", lambda t: y[:, t, :], NODES_READY["t0"])
            products("n0", HID, 1, hT_tile, lambda k: W0[:, 0, :], t_ready("t0"))
            products("s0", HID, 1, hT_tile, lambda k: W0[:, 1, :])
            pe.wait_ge(m_evac, 2 + (STAGE["s0"] + 1) * GROUPS)
            sage_steps(0, HID + 1)
            transposes("t1a", lambda t: acc[0:NT, t, 0:P], NODES_READY["t1"])
            transposes("t1b", lambda t: acc[0:NT, t, P:2 * P], NODES_READY["t1"])
            products("n1", HID, 2, hT_tile, lambda k: W1[:, 0, k, :], t_ready("t1b"))
            products("s1", HID, 2, hT_tile, lambda k: W1[:, 1, k, :])
            pe.wait_ge(m_evac, 2 + (STAGE["s1"] + 1) * GROUPS)
            sage_steps(1, HID)
            transposes("t2a", lambda t: acc[0:NT, t, 0:P], NODES_READY["t2"])
            transposes("t2b", lambda t: acc[0:NT, t, P:2 * P], NODES_READY["t2"])
            products("n2", D, 2, hT_tile, lambda k: W2[:, 0, k, :], t_ready("t2b"))
            products("s2", D, 2, hT_tile, lambda k: W2[:, 1, k, :])
            pe.wait_ge(m_evac, 2 + (STAGE["s2"] + 1) * GROUPS)
            sage_steps(2, D)
            transposes("te", lambda t: y[:, t, :], NODES_READY["te"])
            products("emb", D, 1, hT_tile, lambda k: We[:, :], t_ready("te"))

            for l in range(LAYERS):
                pe.wait_ge(layer_w_loaded, (l + 1) * 6 * 16)
                transposes(f"th{l}", lambda t: h[:, t, :], NODES_READY[f"th{l}"])
                products(f"kv{l}", 2 * D, 1, hT_tile,
                         lambda k: Wqkv[:, 0:2, :].rearrange("p a n -> p (a n)"), t_ready(f"th{l}"))
                products(f"q{l}", D, 1, hT_tile, lambda k: Wqkv[:, 2, :])
                pe.wait_ge(m_evac, 2 + (STAGE[f"q{l}"] + 1) * GROUPS)

                def transpose_onehots(half):
                    for j in range(HALF):
                        last = pe.transpose(psOT[:, j, :], onehot[:, half, j, :], ident[:, :])
                    last.then_inc(oT_done, 1)

                def pick_queries(first_step):
                    _, tiles = nc.values_load_multi_w_load_instructions(
                        step_tile[0:1, ds(first_step, HALF)], engines=(PE,), min_val=0, max_val=TILES - 1,
                        skip_runtime_bounds_check_because="step_tile is built in range")
                    for j in range(HALF):
                        last = pe.matmul(psQ[:, j, :], onehotT[:, j, :],
                                         q[:, ds(tiles[j], 1), :].rearrange("p a n -> p (a n)"),
                                         start=True, stop=True)
                    last.then_inc(q_done, 1)

                pe.wait_ge(onehot_ready, (3 + l) * HALVES + 1)
                transpose_onehots(0)
                with pe.Fori(0, ITERS) as it:
                    for half in range(2):
                        n = l * HALVES + it * 2 + half
                        pe.wait_ge(oT_evac, n + l + 1)
                        pe.wait_ge(prod_done, n + 1)
                        pick_queries(it * RING + half * HALF)
                        pe.wait_ge(onehot_ready, 3 * HALVES + n + 2)
                        transpose_onehots(1 - half)
                        pe.wait_ge(msg_ready, n + 1)
                        for j in range(HALF):
                            pe.wait_ge(added, 3 * STEPS + n * HALF + j - 1)
                            last = pe.matmul(psA(j), onehot[:, half, j, :], msg[:, half, j, :],
                                             start=True, stop=True)
                            last.then_inc(summed, 1)
                        pe.wait_ge(summed, 3 * STEPS + n * HALF + HALF)
                        pe.sem_inc(onehot_free, 1)
                pe.wait_ge(oT_evac, (l + 1) * (HALVES + 1))
                transposes(f"ta{l}", lambda t: y[:, t, :], NODES_READY[f"ta{l}"])
                products(f"o{l}", D, 1, hT_tile, lambda k: Wo_s[:, :], t_ready(f"ta{l}"))
                transposes(f"tx{l}", lambda t: hx[:, t, :], NODES_READY[f"tx{l}"])
                for c in range(2):
                    for g in range(GROUPS):
                        n = (l * 2 + c) * GROUPS + g
                        pe.wait_ge(t_evac, (TSTAGE[f"tx{l}"] + 1) * GROUPS)
                        if n > 0:
                            pe.wait_ge(f_evac, n)
                        for j in range(GROUP):
                            last = pe.matmul(psT[:, j, 0:NT], Wf1_s[:, c * P:(c + 1) * P], hT[:, 0, g * GROUP + j, :],
                                             start=True, stop=True)
                        last.then_inc(f_done, 1)
                products(f"f{l}", D, 2, lambda k, t: fT[:, k, t, :], lambda k: Wf2_s[:, k, :],
                         (f_evac, (l * 2 + 1) * GROUPS + 1))
                pe.wait_ge(m_done, (STAGE[f"f{l}"] + 1) * GROUPS)
                pe.sem_inc(layer_w_used, 1)

        @block.vector
        def _(dve):
            chain = [0]

            def link(ins):
                chain[0] += 1
                ins.then_inc(dve_order, 1)
                dve.wait_ge(dve_order, chain[0])

            def bc(ap, shape):
                return ap.to_broadcast(shape)

            dve.memset(edge_i[:, 0, :, :], PAD_DST).then_inc(edges_padded, 1)
            dve.memset(edge_i[:, 1, :, :], 0).then_inc(edges_padded, 1)
            link(dve.memset(ones[:, :], 1.0))
            dve.wait_ge(iota_ready, 3)
            link(dve.tensor_copy(iota_f[:, :], iota_int[:, :]))
            link(dve.tensor_copy(thr[:, :], thr_int[:, :]))
            link(dve.tensor_copy(tcol[:, :], tcol_int[:, :]))
            link(dve.tensor_scalar(ident[:, :], iota_f[:, 0:P], tcol[:, 0:1], None, ALU.is_equal))
            dve.wait_ge(edges_loaded, 6 * 16)
            for n in range(2):
                link(dve.tensor_copy(edge_f[:, n * CH:(n + 1) * CH, :], edge_i[:, n, :, :]))
            for c in range(CH):
                link(dve.tensor_scalar(ge[:, c, :], thr[:, :], edge_f[:, c, 0:1], None, ALU.is_le))
            link(dve.tensor_reduce(key[:, :], ge[:, :, :], axis=AX, op=ALU.add))
            link(dve.tensor_tensor(key[:, :], key[:, :], tcol[:, :], ALU.add))
            link(dve.tensor_scalar(live[:, :], tcol[:, :], 0.0, None, ALU.is_gt))
            link(dve.tensor_tensor(key[:, :], key[:, :], live[:, :], ALU.mult))
            for c in range(CH):
                link(dve.tensor_scalar(hit[:, c, :], iota_f[:, :], key[:, c:c + 1], None, ALU.is_ge))
            dve.sem_inc(hits_ready, 1)
            dve.wait_ge(counts_ready, 1)
            link(dve.tensor_scalar(step_edge, ps[:, 0, 0:STEPS], -1.0, None, ALU.add))
            for c in range(CH):
                link(dve.tensor_scalar(hit[:, c, :], step_edge, tcol[:, c:c + 1], None, ALU.is_equal))
            dve.sem_inc(picks_ready, 1)
            link(dve.tensor_tensor(step_base, iota_f[:, :], step_edge, ALU.subtract))
            link(dve.tensor_copy(step_tile[:, :], step_base))
            link(dve.tensor_scalar(step_base, step_base, float(NT), None, ALU.mult))
            dve.wait_ge(rows_picked, 2)
            link(dve.tensor_copy(step_src[:, :], ps[:, 2, 0:STEPS]))
            link(dve.tensor_tensor(step_dst[:, 0:STEPS], ps[:, 1, 0:STEPS], step_base, ALU.subtract))
            link(dve.tensor_copy(step_dst[:, STEPS:STEPS + HALF], step_dst[:, 0:HALF]))
            link(dve.memset(slots[:, :, HID:WMAX], 1.0))
            dve.sem_inc(table_ready, 1)

            def layer_norm(name, src, dest):
                link(dve.tensor_reduce(col_a[:, :], src, axis=AX, op=ALU.add))
                link(dve.tensor_scalar(col_a[:, :], col_a[:, :], 1.0 / D, None, ALU.mult))
                link(dve.tensor_tensor(dest, src, bc(col_a[:, :].unsqueeze(2), [NT, TILES, D]), ALU.subtract))
                link(dve.tensor_tensor(q[:, :, :], dest, dest, ALU.mult))
                link(dve.tensor_reduce(col_a[:, :], q[:, :, :], axis=AX, op=ALU.add))
                link(dve.tensor_scalar(col_a[:, :], col_a[:, :], 1.0 / D, EPS, ALU.mult, ALU.add))
                dve.sem_inc(var_ready, 1)
                dve.wait_ge(std_ready, LN[name])
                link(dve.reciprocal(col_a[:, :], col_b[:, :]))
                link(dve.tensor_tensor(dest, dest, bc(col_a[:, :].unsqueeze(2), [NT, TILES, D]), ALU.mult))

            def affine(dest, l, kw, kb):
                for k, op in ((kw, ALU.mult), (kb, ALU.add)):
                    link(dve.tensor_tensor(dest, dest, bc(brow[:, l, k, :].unsqueeze(1), [NT, TILES, D]), op))

            def evac(name, dest, w, bias, row_stage=None):
                for g in range(GROUPS):
                    n = STAGE[name] * GROUPS + g
                    dve.wait_ge(m_done, n + 1)
                    if row_stage is not None and (row_stage > 0 or g >= 2):
                        dve.wait_ge(rows_stored[g % 2], stored(row_stage, g) - 32)
                    o = dest(g)
                    if bias is None:
                        dve.tensor_copy(o, psM(n, w)).then_inc(m_evac, 1)
                    else:
                        dve.tensor_tensor(o, psM(n, w), bc(bias.unsqueeze(1), [NT, GROUP, w]), ALU.add).then_inc(m_evac, 1)
                dve.wait_ge(m_evac, 2 + (STAGE[name] + 1) * GROUPS)

            def to_rows(w):
                return lambda g: G[:, g % 2, :, 0:w]

            def to_nodes(a, w):
                return lambda g: a[:, g * GROUP:(g + 1) * GROUP, 0:w]

            def build_onehots(half, first_step):
                return dve.tensor_tensor(
                    onehot[:, half, :, :],
                    bc(iota_f[:, 0:NT].unsqueeze(1), [P, HALF, NT]),
                    bc(step_dst[:, ds(first_step, HALF)].unsqueeze(2), [P, HALF, NT]), ALU.is_equal)

            def add_half(first_step, bank, w, count, onehot_turn):
                _, tiles = nc.values_load_multi_w_load_instructions(
                    step_tile[0:1, ds(first_step, HALF)], engines=(DVE,), min_val=0, max_val=TILES - 1,
                    skip_runtime_bounds_check_because="step_tile is built in range")
                for j in range(HALF):
                    a = acc[0:NT, ds(tiles[j], 1), 0:w].rearrange("p a n -> p (a n)")
                    dve.wait_ge(summed, count + j + 1)
                    dve.wait_ge(added, count + j + 2)
                    dve.tensor_tensor(a, a, bank(j), ALU.add).then_inc(added, 1)

            def sage_steps(s, w):
                link(dve.memset(acc[:, :, :], 0.0))
                with dve.Fori(0, ITERS) as it:
                    for half in range(2):
                        m = s * HALVES + it * 2 + half
                        dve.wait_ge(onehot_free, m + 2)
                        build_onehots(1 - half, it * RING + (half + 1) * HALF).then_inc(onehot_ready, 1)
                        add_half(it * RING + half * HALF, lambda j: ps[0:NT, 2 + j % 2, 0:w], w,
                                 s * STEPS + it * RING + half * HALF, m)
                dve.wait_ge(added, 2 + (s + 1) * STEPS)

            def combine(w):
                for t in range(TILES):
                    last = dve.scalar_tensor_tensor(acc[0:NT, t, 0:w], acc[0:NT, t, 0:w], inv_deg[:, t:t + 1],
                                                    S[:, t, 0:w], ALU.mult, ALU.add)
                link(last)

            dve.wait_ge(x_loaded, 32)
            layer_norm("ln0", xs[:, :, :], y[:, :, :])
            dve.sem_inc(nodes_ready, 1)
            dve.wait_ge(bias_loaded, 16 * (3 + 11 * LAYERS))
            evac("n0", to_rows(HID), HID, None, 0)
            evac("s0", to_nodes(S, HID), HID, bias_s[:, 0, :])
            build_onehots(0, 0).then_inc(onehot_ready, 1)
            sage_steps(0, HID + 1)
            deg = acc[0:NT, :, HID]
            link(dve.tensor_scalar(col_a[:, :], deg, 1.0, None, ALU.max))
            link(dve.reciprocal(inv_deg[:, :], col_a[:, :]))
            link(dve.tensor_scalar(col_a[:, :], deg, 0.0, None, ALU.is_gt))
            link(dve.tensor_tensor(inv_deg[:, :], inv_deg[:, :], col_a[:, :], ALU.mult))
            combine(HID)
            dve.sem_inc(nodes_ready, 1)
            evac("n1", to_rows(HID), HID, None, 1)
            evac("s1", to_nodes(S, HID), HID, bias_s[:, 1, :])
            sage_steps(1, HID)
            combine(HID)
            dve.sem_inc(nodes_ready, 1)
            evac("n2", to_rows(D), D, None, 2)
            evac("s2", to_nodes(S, D), D, bias_n[:, :])
            sage_steps(2, D)
            combine(D)
            link(dve.scalar_tensor_tensor(xs[:, :, :], acc[0:NT, :, 0:D], 0.0, xs[:, :, :], ALU.max, ALU.add))
            layer_norm("lne", xs[:, :, :], y[:, :, :])
            dve.sem_inc(nodes_ready, 1)
            evac("emb", to_nodes(h, D), D, None)

            for l in range(LAYERS):
                dve.sem_inc(nodes_ready, 1)
                evac(f"kv{l}", to_rows(2 * D), 2 * D,
                     brow[:, l, 0:2, :].rearrange("p a n -> p (a n)"), 3 + l)
                evac(f"q{l}", to_nodes(q, D), D, brow[:, l, 2, :])
                if l == 0:
                    dve.sem_inc(prod_done, 1)
                link(dve.memset(acc[:, :, :], 0.0))
                first = 3 * STEPS + l * STEPS
                with dve.Fori(0, ITERS) as it:
                    for half in range(2):
                        m = l * HALVES + it * 2 + half
                        lo = half * HALF
                        dve.wait_ge(onehot_free, 3 * HALVES + m + 2)
                        build_onehots(1 - half, it * RING + (half + 1) * HALF).then_inc(onehot_ready, 1)
                        dve.wait_ge(q_done, m + 1)
                        for j in range(HALF):
                            dve.wait_ge(gathered[lo + j], ((3 + l) * ITERS + it + 1) * 16)
                        dve.scalar_tensor_tensor(prod[:, :, :], slots[:, lo:lo + HALF, 0:D], DH ** -0.5, psQ,
                                                 ALU.mult, ALU.mult).then_inc(prod_done, 1)
                        dve.wait_ge(prod_done, m + 2)
                        dve.tensor_reduce(score[:, :, :],
                                          prod[:, :, :].rearrange("p j (h e) -> p j h e", h=HEADS),
                                          axis=AX, op=ALU.add).then_inc(score_done, 1)
                        dve.wait_ge(score_done, m + 1)
                        dve.tensor_scalar(clipped[:, :, :], score[:, :, :], -5.0, 5.0, ALU.max, ALU.min)\
                           .then_inc(clip_done, 1)
                        dve.wait_ge(exp_done, m + 1)
                        dve.tensor_tensor(
                            msg[:, half, :, 0:D].rearrange("p j (h e) -> p j h e", h=HEADS),
                            slots[:, lo:lo + HALF, D:2 * D].rearrange("p j (h e) -> p j h e", h=HEADS),
                            bc(msg[:, half, :, D:MW].unsqueeze(3), [P, HALF, HEADS, DH]), ALU.mult)\
                           .then_inc(msg_ready, 1)
                        dve.wait_ge(msg_ready, m + 1)
                        dve.sem_inc(half_free, 1)
                        add_half(it * RING + lo, psA, MW, first + it * RING + lo, m)
                dve.wait_ge(added, 2 + first + STEPS)
                link(dve.tensor_scalar(zr[:, :, :], acc[0:NT, :, D:MW], Z_EPS, None, ALU.add))
                link(dve.reciprocal(zr[:, :, :], zr[:, :, :]))
                link(dve.tensor_tensor(
                    y[:, :, :].rearrange("p t (h e) -> p t h e", h=HEADS),
                    acc[0:NT, :, 0:D].rearrange("p t (h e) -> p t h e", h=HEADS),
                    bc(zr[:, :, :].unsqueeze(3), [NT, TILES, HEADS, DH]), ALU.mult))
                dve.sem_inc(nodes_ready, 1)
                evac(f"o{l}", to_nodes(hx, D), D, brow[:, l, 3, :])
                link(dve.tensor_tensor(hx, hx, h, ALU.add))
                layer_norm(f"ln1_{l}", hx, hx)
                affine(hx, l, 5, 6)
                dve.sem_inc(nodes_ready, 1)
                evac(f"f{l}", to_nodes(h, D), D, brow[:, l, 4, :])
                link(dve.tensor_tensor(h, h, hx, ALU.add))
                layer_norm(f"ln2_{l}", h, h)
                affine(h, l, 7, 8)
            link(dve.tensor_tensor(y[:, :, :], xs[:, :, :], h, ALU.add))
            dve.sem_inc(out_ready, 1)


_INS = ['x', 'src', 'dst', 'L0_gnn_Ws0', 'L0_gnn_Wn0', 'L0_gnn_b0', 'L0_gnn_Ws1', 'L0_gnn_Wn1', 'L0_gnn_b1',
        'L0_gnn_Ws2', 'L0_gnn_Wn2', 'L0_gnn_b2', 'L1_gnn_W_emb', 'L1_gnn_Wq', 'L1_gnn_bq', 'L1_gnn_Wk', 'L1_gnn_bk',
        'L1_gnn_Wv', 'L1_gnn_bv', 'L1_gnn_Wo', 'L1_gnn_bo', 'L1_gnn_ln1_w', 'L1_gnn_ln1_b', 'L1_gnn_Wf1',
        'L1_gnn_bf1', 'L1_gnn_Wf2', 'L1_gnn_bf2', 'L1_gnn_ln2_w', 'L1_gnn_ln2_b']
_OUTS = [((3125, 128), 'float32')]


def kernel(**inputs):
    import numpy as _np
    import concourse.bacc as _bacc
    from concourse import mybir as _mybir
    from concourse.bass_utils import run_bass_kernel_spmd as _run

    nc = _bacc.Bacc("TRN2", target_bir_lowering=False, num_devices=1)
    arrays, args = {}, []
    for name in _INS:
        a = _np.ascontiguousarray(inputs[name])
        arrays[f"in_{name}_dram"] = a
        args.append(nc.dram_tensor(f"in_{name}_dram", a.shape, _mybir.dt.from_np(a.dtype), kind="ExternalInput").ap())
    for i, (shape, dtype) in enumerate(_OUTS):
        dt = _mybir.dt.from_np(_np.dtype(dtype))
        args.append(nc.dram_tensor(f"out_{i}_dram", shape, dt, kind="ExternalOutput").ap())
    gnn_kernel(nc, *args)
    r = _run(nc, [arrays], core_ids=[0])
    return r.results[0]["out_0_dram"]
```

```python
import concourse.bass as bass
from concourse import mybir
from contextlib import ExitStack


def gnn_kernel(nc, x, src, dst, Ws0, Wn0, b0, Ws1, Wn1, b1, Ws2, Wn2, b2, W_emb, Wq, bq, Wk, bk, Wv, bv,
               Wo, bo, ln1_w, ln1_b, Wf1, bf1, Wf2, bf2, ln2_w, ln2_b, out):
    fp32 = mybir.dt.float32
    i32 = mybir.dt.int32
    ALU = mybir.AluOpType
    ACT = mybir.ActivationFunctionType
    AX = mybir.AxisListType.X
    DVE, PE = mybir.EngineType.DVE, mybir.EngineType.PE
    ds = bass.ds

    NODES, D = x.shape
    EDGES = src.shape[0]
    HID = Ws0.shape[1]
    LAYERS = Wq.shape[0]
    HEADS = 8
    DH = D // HEADS
    P = 128
    NT = 125
    TILES = NODES // NT
    GROUP = 4
    GR = [(t, min(t + GROUP, TILES)) for t in range(0, TILES, GROUP)]
    NG = len(GR)
    ETILES = -(-EDGES // P)
    CH = -(-ETILES // P)
    HALF = 8
    RING = 2 * HALF
    STEPS = -(-(ETILES + TILES - 1) // RING) * RING
    ITERS = STEPS // RING
    HALVES = STEPS // HALF
    SAGE = 3
    WMAX = HID + 1
    MW = D + HEADS
    PAD_DST = 1000000
    EPS = 1e-5
    Z_EPS = 1e-6
    SPLIT = NT // 16 * 16

    rows_w = nc.dram_tensor("rows_w", [NODES, HID], fp32, kind="Internal").ap()
    rows_n = nc.dram_tensor("rows_n", [NODES, D], fp32, kind="Internal").ap()
    rows_w_t = rows_w.rearrange("(t p) w -> p t w", p=NT)
    rows_n_t = rows_n.rearrange("(t p) w -> p t w", p=NT)
    x_t = x.rearrange("(t p) w -> p t w", p=NT)
    out_t = out.rearrange("(t p) w -> p t w", p=NT)

    with ExitStack() as ctx:
        def sb(name, shape, dt=fp32):
            return ctx.enter_context(nc.sbuf_tensor(name, shape, dt))

        def sem(name):
            return ctx.enter_context(nc.semaphore(name))

        iota_int = sb("iota_int", [P, STEPS], i32)
        thr_int = sb("thr_int", [P, TILES - 1], i32)
        tcol_int = sb("tcol_int", [P, CH], i32)
        iota_f = sb("iota_f", [P, STEPS])
        thr = sb("thr", [P, TILES - 1])
        tcol = sb("tcol", [P, CH])
        ident = sb("ident", [P, P])
        ones = sb("ones", [P, P])
        step_src = sb("step_src", [P, STEPS], i32)
        step_dst = sb("step_dst", [P, STEPS + HALF])
        step_tile = sb("step_tile", [P, STEPS + HALF], i32)
        idx_ring = sb("idx_ring", [P, 2, HALF], i32)
        xs = sb("xs", [NT, TILES, D])
        S = sb("S", [NT, TILES, HID])
        h = S[:, :, 0:D]
        hx = S[:, :, D:2 * D]
        acc = sb("acc", [P, TILES, WMAX])
        y = sb("y", [NT, TILES, D])
        q = sb("q", [NT, TILES, D])
        rows_out = sb("rows_out", [NT, 2, GROUP, HID])
        hT = sb("hT", [P, 2, TILES, NT])
        fT = sb("fT", [P, 2, 2, GROUP, NT])
        inv_deg = sb("inv_deg", [NT, TILES])
        deg_pos = sb("deg_pos", [NT, TILES])
        stats = sb("stats", [NT, TILES, 6])
        mean_var = sb("mean_var", [NT, TILES, 2])
        eps_col = sb("eps_col", [NT, 1])
        rstd = sb("rstd", [NT, TILES])
        zr = sb("zr", [NT, TILES, HEADS])
        W0 = sb("W0", [P, 2, HID])
        W1 = sb("W1", [P, 2, 2, HID])
        W2 = sb("W2", [P, 2, 2, D])
        We = sb("We", [P, D])
        Wqkv = sb("Wqkv", [P, 3, D])
        Wo_s = sb("Wo_s", [P, D])
        Wf1_s = sb("Wf1_s", [P, 2 * D])
        Wf2_s = sb("Wf2_s", [P, 2, D])
        bias_s = sb("bias_s", [NT, 2, HID])
        bias_n = sb("bias_n", [NT, D])
        brow = sb("brow", [NT, LAYERS, 9, D])
        bf1_col = sb("bf1_col", [P, LAYERS, 2])
        slots = sb("slots", [P, RING, WMAX])
        onehot = sb("onehot", [P, 2, HALF, NT])
        onehotT = sb("onehotT", [NT, HALF, P])
        prod = sb("prod", [P, HALF, D])
        score = sb("score", [P, HALF, HEADS])
        clipped = sb("clipped", [P, HALF, HEADS])
        msg = sb("msg", [P, 2, HALF, MW])
        edge_i = msg[:, :, :, :].rearrange("p a j n -> p (a j n)")[:, 0:2 * CH * P].bitcast(i32).rearrange(
            "p (a c e) -> p a c e", a=2, c=CH)
        edge_f = slots[:, 0:2 * CH, 0:P]
        acc_flat = acc[:, :, :].rearrange("p t w -> p (t w)")
        hit = acc_flat[:, 0:CH * STEPS].rearrange("p (c s) -> p c s", c=CH)
        step_edge = acc_flat[:, CH * STEPS:(CH + 1) * STEPS]
        step_base = acc_flat[:, (CH + 1) * STEPS:(CH + 2) * STEPS]
        ge = sb("ge", [P, CH, TILES - 1])
        key = sb("key", [P, CH])
        live = sb("live", [P, CH])

        ps = ctx.enter_context(nc.psum_tensor("ps", [P, 8, 512], fp32))
        flat = ps[:, :, :].rearrange("p b n -> p (b n)")

        def psT(n, tiles):
            return ps[:, n % 2, 0:tiles * NT].rearrange("p (j n) -> p j n", j=tiles)

        def psM(n, w, tiles):
            o = 1024 + 1024 * (n % 3)
            return flat[0:NT, o:o + tiles * w].rearrange("p (j n) -> p j n", j=tiles)

        psOT = flat[0:NT, 0:HALF * P].rearrange("p (j n) -> p j n", j=HALF)
        psQ = flat[:, 1024:1024 + HALF * D].rearrange("p (j n) -> p j n", j=HALF)

        def psA(j):
            return ps[0:NT, 4 + j // 2, (j % 2) * MW:(j % 2 + 1) * MW]

        def waves(*stages):
            return [(name, w - lag) for w in range(NG + max(lag for _, lag in stages))
                    for name, lag in stages if 0 <= w - lag < NG]

        LAYER_WAVES = []
        for l in range(LAYERS):
            st = [(f"o{l}", 0), (f"f{l}", 1)]
            if l + 1 < LAYERS:
                st.append((f"kv{l + 1}", 2))
            LAYER_WAVES.append(waves(*st))
        ENTRY_WAVES = waves(("emb", 0), ("kv0", 1))
        T_PARTS = {"n0": ["t0"], "n1": ["t1a", "t1b"], "n2": ["t2a", "t2b"], "emb": ["te"]}
        for l in range(LAYERS):
            T_PARTS[f"kv{l}"] = [f"th{l}"]
            T_PARTS[f"o{l}"] = [f"ta{l}"]
            T_PARTS[f"f{l}"] = [f"tx{l}", f"f1a{l}", f"f1b{l}"]
        M_ORDER, T_ORDER = [], []
        for s in range(SAGE):
            T_ORDER += [(t, g) for g in range(NG) for t in T_PARTS[f"n{s}"]]
            M_ORDER += [(f"n{s}", g) for g in range(NG)] + [(f"s{s}", g) for g in range(NG)]
        plan = [ENTRY_WAVES + [("q0", g) for g in range(NG)]]
        for l in range(LAYERS):
            plan.append(LAYER_WAVES[l] + ([(f"q{l + 1}", g) for g in range(NG)] if l + 1 < LAYERS else []))
        for part in plan:
            for name, g in part:
                T_ORDER += [(t, g) for t in T_PARTS.get(name, [])]
                M_ORDER.append((name, g))
        LN_ORDER = [("x", g) for g in range(NG)] + [("x2", g) for g in range(NG)]
        for l in range(LAYERS):
            LN_ORDER += waves((f"hx{l}", 0), (f"h{l}", 1))
        LN_UNIT = {u: n for n, u in enumerate(LN_ORDER)}
        M_UNIT = {u: n for n, u in enumerate(M_ORDER)}
        T_UNIT = {u: n for n, u in enumerate(T_ORDER)}
        ROW_STAGES = [("n0", HID), ("n1", HID), ("n2", D)] + [(f"kv{l}", 2 * D) for l in range(LAYERS)]

        def stored(s, g):
            per = len(range(g % 2, NG, 2))
            return (s * per + g // 2 + 1) * 32

        iota_ready = sem("iota_ready")
        edges_padded = sem("edges_padded")
        edges_loaded = sem("edges_loaded")
        x_loaded = sem("x_loaded")
        w_loaded = sem("w_loaded")
        bias_loaded = sem("bias_loaded")
        layer_w_loaded = sem("layer_w_loaded")
        hits_ready = sem("hits_ready")
        counts_ready = sem("counts_ready")
        picks_ready = sem("picks_ready")
        rows_picked = sem("rows_picked")
        table_ready = sem("table_ready")
        dve_order = sem("dve_order")
        eps_ready = sem("eps_ready")
        var_ready = sem("var_ready")
        std_ready = sem("std_ready")
        y_ready = sem("y_ready")
        comb_ready = sem("comb_ready")
        hx_ready = sem("hx_ready")
        h_ready = sem("h_ready")
        x_summed = sem("x_summed")
        h_biased = sem("h_biased")
        hx_biased = sem("hx_biased")
        t_done = sem("t_done")
        t_evac = sem("t_evac")
        m_done = sem("m_done")
        m_evac = sem("m_evac")
        acc_zeroed = sem("acc_zeroed")
        rows_stored = [sem("rows_stored_a"), sem("rows_stored_b")]
        pool_step = sem("pool_step")
        idx_copied = sem("idx_copied")
        gathered = [sem(f"gathered{b}") for b in range(RING)]
        half_free = sem("half_free")
        onehot_ready = sem("onehot_ready")
        onehot_free = sem("onehot_free")
        summed = sem("summed")
        added = sem("added")
        oT_done = sem("oT_done")
        oT_evac = sem("oT_evac")
        q_done = sem("q_done")
        prod_done = sem("prod_done")
        score_done = sem("score_done")
        clip_done = sem("clip_done")
        exp_done = sem("exp_done")
        msg_ready = sem("msg_ready")
        out_ready = sem("out_ready")
        out_stored = sem("out_stored")

        block = ctx.enter_context(nc.Block())

        @block.sync
        def _(sp):
            for lo, hi in ((0, SPLIT), (SPLIT, NT)):
                sp.dma_start(xs[lo:hi, :, :], x_t[lo:hi]).then_inc(x_loaded, 16)
            sp.wait_ge(edges_padded, 2)
            full = EDGES // P
            whole = (CH - 1) * P
            for n, a in enumerate((dst, src)):
                sp.dma_start(edge_i[:, n, 0:CH - 1, :],
                             a[0:whole * P].rearrange("(c p e) -> p c e", p=P, e=P)).then_inc(edges_loaded, 16)
                sp.dma_start(edge_i[0:full - whole, n, CH - 1, :],
                             a[whole * P:full * P].rearrange("(p e) -> p e", e=P)).then_inc(edges_loaded, 16)
                sp.dma_start(edge_i[full - whole:full - whole + 1, n, CH - 1, 0:EDGES - full * P],
                             a[full * P:EDGES].rearrange("(p e) -> p e", p=1)).then_inc(edges_loaded, 16)
            for a, b in ((W0[:, 0, :], Wn0), (W0[:, 1, :], Ws0),
                         (W1[:, 0, :, :], Wn1.rearrange("(k p) n -> p k n", p=P)),
                         (W1[:, 1, :, :], Ws1.rearrange("(k p) n -> p k n", p=P)),
                         (W2[:, 0, :, :], Wn2.rearrange("(k p) n -> p k n", p=P)),
                         (W2[:, 1, :, :], Ws2.rearrange("(k p) n -> p k n", p=P)),
                         (We[:, :], W_emb)):
                sp.dma_start(a, b).then_inc(w_loaded, 16)
            for name, w in ROW_STAGES:
                dram = rows_n_t if w == D else rows_w_t
                for g, (t0, t1) in enumerate(GR):
                    sp.wait_ge(m_evac, 3 + M_UNIT[(name, g)] + 1)
                    for lo, hi in ((0, SPLIT), (SPLIT, NT)):
                        sp.dma_start(dram[lo:hi, t0:t1, :],
                                     rows_out[lo:hi, g % 2, 0:t1 - t0, 0:w]).then_inc(rows_stored[g % 2], 16)
            for g, (t0, t1) in enumerate(GR):
                sp.wait_ge(out_ready, g + 1)
                for lo, hi in ((0, SPLIT), (SPLIT, NT)):
                    sp.dma_start(out_t[lo:hi, t0:t1, :], y[lo:hi, t0:t1, :]).then_inc(out_stored, 16)
            sp.wait_ge(out_stored, 32 * NG)

        @block.gpsimd
        def _(pool):
            pool.iota(iota_int[:, :], pattern=[[1, STEPS]], base=0, channel_multiplier=0).then_inc(iota_ready, 1)
            pool.iota(thr_int[:, :], pattern=[[NT, TILES - 1]], base=NT, channel_multiplier=0).then_inc(iota_ready, 1)
            pool.iota(tcol_int[:, :], pattern=[[P, CH]], base=0, channel_multiplier=1).then_inc(iota_ready, 1)

            def bias_feed_forward(l):
                for g, (t0, t1) in enumerate(GR):
                    pool.wait_ge(hx_ready, l * NG + g + 1)
                    bf2_row = brow[:, l, 4, :].unsqueeze(1).to_broadcast([NT, t1 - t0, D])
                    pool.tensor_tensor(y[:, t0:t1, :], hx[:, t0:t1, :], bf2_row, ALU.add).then_inc(hx_biased, 1)

            for s, (name, w) in enumerate(ROW_STAGES):
                if s > SAGE:
                    bias_feed_forward(s - SAGE - 1)
                if s == 0:
                    pool.wait_ge(table_ready, 1)
                elif s < SAGE:
                    pool.wait_ge(t_done, T_UNIT[(f"t{s}b", NG - 1)] + 1)
                elif s == SAGE:
                    pool.wait_ge(x_summed, 1)
                else:
                    pool.wait_ge(y_ready, NG * (2 + s - SAGE))
                pool.memset(acc[:, :, :], 0.0).then_inc(acc_zeroed, 1)
                for b in range(2):
                    pool.wait_ge(rows_stored[b], stored(s, max(g for g in range(NG) if g % 2 == b)))
                rows = rows_n if w == D else rows_w
                with pool.Fori(0, ITERS) as it:
                    for half in range(2):
                        pool.wait_ge(half_free, s * HALVES + it * 2 + half + 1)
                        pool.sem_inc(pool_step, 1)
                        pool.tensor_copy(idx_ring[:, half, :],
                                         step_src[:, ds(it * RING + half * HALF, HALF)]).then_inc(idx_copied, 1)
                        pool.wait_ge(idx_copied, s * HALVES + it * 2 + half + 1)
                        pool.sem_inc(pool_step, 1)
                        for j in range(HALF):
                            b = half * HALF + j
                            pool.indirect_dma_start(
                                out=slots[:, b, 0:w], out_offset=None, in_=rows,
                                in_offset=bass.IndirectOffsetOnAxis(ap=idx_ring[:, half, j:j + 1], axis=0),
                            ).then_inc(gathered[b], 16)
                if s >= SAGE:
                    if s == SAGE:
                        pool.wait_ge(bias_loaded, 16 * (3 + 11 * LAYERS))
                    bo_row = brow[:, s - SAGE, 3, :].unsqueeze(1).to_broadcast([NT, TILES, D])
                    pool.tensor_tensor(h, h, bo_row, ALU.add).then_inc(h_biased, 1)
            bias_feed_forward(LAYERS - 1)

        @block.scalar
        def _(act):
            def row(v):
                return v.rearrange("(a n) -> a n", a=1).to_broadcast([NT, v.shape[0]])
            vectors = [(bias_s[:, 0, :], row(b0)), (bias_s[:, 1, :], row(b1)), (bias_n[:, :], row(b2))]
            for l in range(LAYERS):
                for k, v in enumerate((bk, bv, bq, bo, bf2, ln1_w, ln1_b, ln2_w, ln2_b)):
                    vectors.append((brow[:, l, k, :], row(v[l])))
                for c in range(2):
                    vectors.append((bf1_col[:, l, c:c + 1],
                                    bf1[l, c * P:(c + 1) * P].rearrange("(p a) -> p a", a=1)))
            for a, b in vectors:
                act.dma_start(a, b).then_inc(bias_loaded, 16)

            def load_layer(parts):
                for a, b in parts:
                    act.dma_start(a, b).then_inc(layer_w_loaded, 16)

            def attention_in(l):
                return ((Wqkv[:, 0, :], Wk[l]), (Wqkv[:, 1, :], Wv[l]), (Wqkv[:, 2, :], Wq[l]))

            def attention_out(l):
                return ((Wo_s[:, :], Wo[l]), (Wf1_s[:, :], Wf1[l]),
                        (Wf2_s[:, :, :], Wf2[l].rearrange("(k p) n -> p k n", p=P)))

            load_layer(attention_in(0) + attention_out(0))

            def evac_t(name, g):
                n = T_UNIT[(name, g)]
                t0, t1 = GR[g]
                act.wait_ge(t_done, n + 1)
                if name[:2] == "f1":
                    l, c = int(name[3:]), "ab".index(name[2])
                    if (l, g) > (0, 1):
                        act.wait_ge(m_done, M_UNIT[(f"f{l}", g - 2) if g >= 2 else (f"f{l - 1}", NG - 2 + (g + NG) % 2)] + 1)
                    act.activation(fT[:, c, g % 2, 0:t1 - t0, :], psT(n, t1 - t0), ACT.Relu,
                                   bias=bf1_col[:, l, c:c + 1]).then_inc(t_evac, 1)
                else:
                    k = 1 if name[-1] == "b" else 0
                    func = ACT.Relu if name[:2] in ("t0", "t1", "t2", "te") else ACT.Copy
                    act.activation(hT[:, k, t0:t1, :], psT(n, t1 - t0), func).then_inc(t_evac, 1)

            def evac_part(stages):
                for t, g in T_ORDER:
                    if t in stages:
                        evac_t(t, g)

            def std(unit, g):
                t0, t1 = GR[g]
                act.wait_ge(var_ready, LN_UNIT[(unit, g)] + 1)
                act.activation(rstd[:, t0:t1], mean_var[:, t0:t1, 1], ACT.Sqrt, bias=eps_col[:, 0:1])\
                   .then_inc(std_ready, 1)

            act.wait_ge(eps_ready, 1)
            for w in range(NG + 1):
                if w < NG:
                    std("x", w)
                if w > 0:
                    evac_t("t0", w - 1)
            act.wait_ge(bias_loaded, 16 * (3 + 11 * LAYERS))
            evac_part(("t1a", "t1b"))
            evac_part(("t2a", "t2b"))
            for w in range(NG + 1):
                if w < NG:
                    std("x2", w)
                    evac_t("te", w)
                if w > 0:
                    evac_t("th0", w - 1)
            for l in range(LAYERS):
                if l > 0:
                    act.wait_ge(m_done, M_UNIT[(f"f{l - 1}", NG - 1)] + 1)
                    load_layer(attention_out(l))
                if l + 1 < LAYERS:
                    act.wait_ge(m_done, M_UNIT[(f"q{l}", NG - 1)] + 1)
                    load_layer(attention_in(l + 1))

                act.wait_ge(oT_done, l * (HALVES + 1) + 1)
                act.activation(onehotT[:, :, :], psOT, ACT.Copy).then_inc(oT_evac, 1)
                with act.Fori(0, ITERS) as it:
                    for half in range(2):
                        n = l * HALVES + it * 2 + half
                        act.wait_ge(clip_done, n + 1)
                        act.wait_ge(onehot_free, SAGE * HALVES + n + 1)
                        act.activation(msg[:, half, :, D:MW], clipped[:, :, :], ACT.Exp).then_inc(exp_done, 1)
                        act.wait_ge(oT_done, n + l + 2)
                        act.wait_ge(q_done, n + l + 1)
                        act.activation(onehotT[:, :, :], psOT, ACT.Copy).then_inc(oT_evac, 1)
                for w in range(NG + 2):
                    if w < NG:
                        evac_t(f"ta{l}", w)
                    if 0 <= w - 1 < NG:
                        std(f"hx{l}", w - 1)
                    if 0 <= w - 2 < NG:
                        std(f"h{l}", w - 2)
                    if 0 <= w - 1 < NG:
                        for t in (f"tx{l}", f"f1a{l}", f"f1b{l}"):
                            evac_t(t, w - 1)
                    if l + 1 < LAYERS and 0 <= w - 2 < NG:
                        evac_t(f"th{l + 1}", w - 2)

        @block.tensor
        def _(pe):
            pe.sem_inc(half_free, 2)
            pe.sem_inc(onehot_free, 2)
            pe.sem_inc(added, 2)
            pe.sem_inc(t_evac, 2)
            pe.sem_inc(m_evac, 3)

            def transposes(name, g, src_tile):
                n = T_UNIT[(name, g)]
                t0, t1 = GR[g]
                pe.wait_ge(t_evac, n + 1)
                for t in range(t0, t1):
                    last = pe.transpose(psT(n, t1 - t0)[:, t - t0, :], src_tile(t), ident[0:NT, 0:NT])
                last.then_inc(t_done, 1)

            def products(name, g, w, kk, operand, weight, reads=None):
                n = M_UNIT[(name, g)]
                t0, t1 = GR[g]
                pe.wait_ge(m_evac, n + 1)
                if reads:
                    pe.wait_ge(t_evac, 2 + T_UNIT[(reads, g)] + 1)
                for t in range(t0, t1):
                    for k in range(kk):
                        last = pe.matmul(psM(n, w, t1 - t0)[:, t - t0, :], operand(k, t), weight(k),
                                         start=k == 0, stop=k == kk - 1)
                last.then_inc(m_done, 1)

            def hT_tile(k, t):
                return hT[:, k, t, :]

            def sage_steps(s, w):
                with pe.Fori(0, ITERS) as it:
                    for half in range(2):
                        pe.wait_ge(onehot_ready, s * HALVES + it * 2 + half + 1)
                        for j in range(HALF):
                            n = s * STEPS + it * RING + half * HALF + j
                            b = half * HALF + j
                            pe.wait_ge(added, n + 1)
                            pe.wait_ge(gathered[b], (s * ITERS + it + 1) * 16)
                            pe.matmul(ps[0:NT, j % 2, 0:w], onehot[:, half, j, :], slots[:, b, 0:w],
                                      start=True, stop=True).then_inc(summed, 1)
                        pe.wait_ge(summed, s * STEPS + it * RING + half * HALF + HALF)
                        pe.sem_inc(half_free, 1)
                        pe.sem_inc(onehot_free, 1)

            table_1, table_2 = 3, 5
            pe.wait_ge(y_ready, 1)
            for g in range(NG):
                pe.wait_ge(y_ready, g + 1)
                transposes("t0", g, lambda t: y[:, t, :])
                if g == 0:
                    pe.wait_ge(w_loaded, 7 * 16)
                if g < table_1:
                    products("n0", g, HID, 1, hT_tile, lambda k: W0[:, 0, :], "t0")
            pe.wait_ge(t_evac, 2 + NG)
            for g in range(table_1, NG):
                if g == table_1:
                    pe.wait_ge(hits_ready, 1)
                    for c in range(CH):
                        last = pe.matmul(ps[:, 0, 0:STEPS], ones[:, :], hit[:, c, :], start=c == 0, stop=c == CH - 1)
                    last.then_inc(counts_ready, 1)
                if g == table_2:
                    pe.wait_ge(picks_ready, 1)
                    for n in range(2):
                        for c in range(CH):
                            last = pe.matmul(ps[:, n, 0:STEPS], edge_f[:, n * CH + c, :], hit[:, c, :],
                                             start=c == 0, stop=c == CH - 1)
                        last.then_inc(rows_picked, 1)
                products("n0", g, HID, 1, hT_tile, lambda k: W0[:, 0, :], "t0")
            for g in range(NG):
                products("s0", g, HID, 1, hT_tile, lambda k: W0[:, 1, :])
            pe.wait_ge(table_ready, 1)
            sage_steps(0, HID + 1)
            for s, W, w in ((1, W1, HID), (2, W2, D)):
                for g in range(NG + 1):
                    if g < NG:
                        pe.wait_ge(comb_ready, (s - 1) * NG + g + 1)
                        for k in range(2):
                            transposes(f"t{s}{'ab'[k]}", g, lambda t: acc[0:NT, t, k * P:(k + 1) * P])
                    if g > 0:
                        products(f"n{s}", g - 1, w, 2, hT_tile, lambda k: W[:, 0, k, :], f"t{s}b")
                for g in range(NG):
                    products(f"s{s}", g, w, 2, hT_tile, lambda k: W[:, 1, k, :])
                pe.wait_ge(t_evac, 2 + T_UNIT[(f"t{s}b", NG - 1)] + 1)
                sage_steps(s, w)

            def node_wave(name, g):
                stage, l = (name, 0) if name == "emb" else (name[:-1], int(name[-1]))
                if stage == "emb":
                    pe.wait_ge(y_ready, NG + g + 1)
                    transposes("te", g, lambda t: y[:, t, :])
                    products(name, g, D, 1, hT_tile, lambda k: We[:, :], "te")
                elif stage == "kv":
                    pe.wait_ge(h_ready, l * NG + g + 1)
                    if g == 0:
                        pe.wait_ge(layer_w_loaded, 16 * (6 if l == 0 else 6 * l + 3))
                    transposes(f"th{l}", g, lambda t: h[:, t, :])
                    products(name, g, 2 * D, 1, hT_tile,
                             lambda k: Wqkv[:, 0:2, :].rearrange("p a n -> p (a n)"), f"th{l}")
                elif stage == "q":
                    products(name, g, D, 1, hT_tile, lambda k: Wqkv[:, 2, :])
                elif stage == "o":
                    pe.wait_ge(y_ready, (2 + l) * NG + g + 1)
                    if g == 0:
                        pe.wait_ge(layer_w_loaded, 16 * (6 * (l + 1) + (3 if l + 1 < LAYERS else 0)))
                    transposes(f"ta{l}", g, lambda t: y[:, t, :])
                    products(name, g, D, 1, hT_tile, lambda k: Wo_s[:, :], f"ta{l}")
                elif stage == "f":
                    pe.wait_ge(hx_ready, l * NG + g + 1)
                    transposes(f"tx{l}", g, lambda t: hx[:, t, :])
                    t0, t1 = GR[g]
                    for c in range(2):
                        n = T_UNIT[(f"f1{'ab'[c]}{l}", g)]
                        pe.wait_ge(t_evac, max(n + 1, 2 + T_UNIT[(f"tx{l}", g)] + 1))
                        last = pe.matmul(ps[:, n % 2, 0:(t1 - t0) * NT], Wf1_s[:, c * P:(c + 1) * P],
                                         hT[:, 0, t0:t1, :].rearrange("p t n -> p (t n)"), start=True, stop=True)
                        last.then_inc(t_done, 1)
                    products(name, g, D, 2, lambda k, t: fT[:, k, g % 2, t - t0, :], lambda k: Wf2_s[:, k, :],
                             f"f1b{l}")

            for name, g in plan[0]:
                node_wave(name, g)
            for l in range(LAYERS):
                pe.wait_ge(m_evac, 3 + M_UNIT[(f"q{l}", NG - 1)] + 1)

                def transpose_onehots(half):
                    for j in range(HALF):
                        last = pe.transpose(psOT[:, j, :], onehot[:, half, j, :], ident[:, :])
                    last.then_inc(oT_done, 1)

                def pick_queries(first_step):
                    _, tiles = nc.values_load_multi_w_load_instructions(
                        step_tile[0:1, ds(first_step, HALF)], engines=(PE,), min_val=0, max_val=TILES - 1,
                        skip_runtime_bounds_check_because="step_tile is built in range")
                    for j in range(HALF):
                        last = pe.matmul(psQ[:, j, :], onehotT[:, j, :],
                                         q[:, ds(tiles[j], 1), :].rearrange("p a n -> p (a n)"),
                                         start=True, stop=True)
                    last.then_inc(q_done, 1)

                pe.wait_ge(onehot_ready, (SAGE + l) * HALVES + 1)
                transpose_onehots(0)
                pe.wait_ge(oT_evac, l * (HALVES + 1) + 1)
                pick_queries(0)
                with pe.Fori(0, ITERS) as it:
                    for half in range(2):
                        n = l * HALVES + it * 2 + half
                        pe.wait_ge(onehot_ready, SAGE * HALVES + n + 2)
                        transpose_onehots(1 - half)
                        pe.wait_ge(oT_evac, n + l + 2)
                        pe.wait_ge(prod_done, n + 1)
                        pick_queries(it * RING + (half + 1) * HALF)
                        pe.wait_ge(msg_ready, n + 1)
                        for j in range(HALF):
                            if j % 2 == 0:
                                pe.wait_ge(added, 2 + SAGE * STEPS + n * HALF + j + 2 - HALF)
                            pe.matmul(psA(j), onehot[:, half, j, :], msg[:, half, j, :],
                                      start=True, stop=True).then_inc(summed, 1)
                        pe.wait_ge(summed, SAGE * STEPS + n * HALF + HALF)
                        pe.sem_inc(onehot_free, 1)
                pe.wait_ge(oT_evac, (l + 1) * (HALVES + 1))
                for name, g in plan[1 + l]:
                    node_wave(name, g)

        @block.vector
        def _(dve):
            chain = [0]

            def link(ins):
                chain[0] += 1
                ins.then_inc(dve_order, 1)
                dve.wait_ge(dve_order, chain[0])

            def bc(ap, shape):
                return ap.to_broadcast(shape)

            def norm_stats(g, src_tile):
                tiles = range(*GR[g])
                for t in tiles:
                    last = dve.bn_stats(stats[:, t, :], src_tile(t))
                link(last)
                for t in tiles:
                    last = dve.bn_aggr(mean_var[:, t, :], stats[:, t, :])
                last.then_inc(var_ready, 1)

            def norm_apply(unit, g, src_tile, dest_tile, l=None, kw=None, kb=None):
                tiles = range(*GR[g])
                t0, t1 = GR[g]
                dve.wait_ge(std_ready, LN_UNIT[(unit, g)] + 1)
                link(dve.reciprocal(rstd[:, t0:t1], rstd[:, t0:t1]))
                if l is None:
                    for t in tiles:
                        last = dve.tensor_scalar(dest_tile(t), src_tile(t), mean_var[:, t, 0:1], rstd[:, t:t + 1],
                                                 ALU.subtract, ALU.mult)
                    return last
                for t in tiles:
                    last = dve.scalar_tensor_tensor(dest_tile(t), src_tile(t), mean_var[:, t, 0:1],
                                                    brow[:, l, kw, :], ALU.subtract, ALU.mult)
                link(last)
                for t in tiles:
                    last = dve.scalar_tensor_tensor(dest_tile(t), dest_tile(t), rstd[:, t:t + 1],
                                                    brow[:, l, kb, :], ALU.mult, ALU.add)
                return last

            def evac(name, g, dest, w, addend=None, row_stage=None):
                n = M_UNIT[(name, g)]
                t0, t1 = GR[g]
                dve.wait_ge(m_done, n + 1)
                if row_stage is not None:
                    dest = rows_out[:, g % 2, 0:t1 - t0, 0:w]
                    if row_stage > 0 or g >= 2:
                        dve.wait_ge(rows_stored[g % 2], stored(row_stage, g) - 32)
                if addend is None:
                    dve.tensor_copy(dest, psM(n, w, t1 - t0)).then_inc(m_evac, 1)
                else:
                    dve.tensor_tensor(dest, psM(n, w, t1 - t0), addend, ALU.add).then_inc(m_evac, 1)

            def row_of(ap, g, w):
                t0, t1 = GR[g]
                return bc(ap.unsqueeze(1), [NT, t1 - t0, w])

            def build_onehots(half, first_step):
                return dve.tensor_tensor(
                    onehot[:, half, :, :],
                    bc(iota_f[:, 0:NT].unsqueeze(1), [P, HALF, NT]),
                    bc(step_dst[:, ds(first_step, HALF)].unsqueeze(2), [P, HALF, NT]), ALU.is_equal)

            def add_half(first_step, bank, w, count, per_bank=1):
                _, tiles = nc.values_load_multi_w_load_instructions(
                    step_tile[0:1, ds(first_step, HALF)], engines=(DVE,), min_val=0, max_val=TILES - 1,
                    skip_runtime_bounds_check_because="step_tile is built in range")
                for j in range(HALF):
                    a = acc[0:NT, ds(tiles[j], 1), 0:w].rearrange("p a n -> p (a n)")
                    dve.wait_ge(summed, count + (j // per_bank + 1) * per_bank)
                    dve.wait_ge(added, count + j + 2)
                    dve.tensor_tensor(a, a, bank(j), ALU.add).then_inc(added, 1)

            def sage_steps(s, w):
                dve.wait_ge(acc_zeroed, s + 1)
                with dve.Fori(0, ITERS) as it:
                    for half in range(2):
                        m = s * HALVES + it * 2 + half
                        dve.wait_ge(onehot_free, m + 2)
                        build_onehots(1 - half, it * RING + (half + 1) * HALF).then_inc(onehot_ready, 1)
                        add_half(it * RING + half * HALF, lambda j: ps[0:NT, j % 2, 0:w], w,
                                 s * STEPS + it * RING + half * HALF)
                dve.wait_ge(added, 2 + (s + 1) * STEPS)

            def combine(g, w):
                for t in range(*GR[g]):
                    last = dve.scalar_tensor_tensor(acc[0:NT, t, 0:w], acc[0:NT, t, 0:w], inv_deg[:, t:t + 1],
                                                    S[:, t, 0:w], ALU.mult, ALU.add)
                return last

            dve.memset(edge_i[:, 0, :, :], PAD_DST).then_inc(edges_padded, 1)
            dve.memset(edge_i[:, 1, :, :], 0).then_inc(edges_padded, 1)
            dve.memset(ones[:, :], 1.0)
            dve.memset(eps_col[:, :], EPS).then_inc(eps_ready, 1)
            dve.wait_ge(iota_ready, 3)
            dve.tensor_copy(iota_f[:, :], iota_int[:, :])
            dve.tensor_copy(thr[:, :], thr_int[:, :])
            link(dve.tensor_copy(tcol[:, :], tcol_int[:, :]))
            link(dve.tensor_scalar(ident[:, :], iota_f[:, 0:P], tcol[:, 0:1], None, ALU.is_equal))
            dve.wait_ge(x_loaded, 32)
            for g in range(NG + 1):
                if g < NG:
                    norm_stats(g, lambda t: xs[:, t, :])
                if g > 0:
                    norm_apply("x", g - 1, lambda t: xs[:, t, :], lambda t: y[:, t, :]).then_inc(y_ready, 1)
            dve.wait_ge(edges_loaded, 6 * 16)
            for n in range(2):
                last = dve.tensor_copy(edge_f[:, n * CH:(n + 1) * CH, :], edge_i[:, n, :, :])
            link(last)
            for c in range(CH):
                last = dve.tensor_scalar(ge[:, c, :], thr[:, :], edge_f[:, c, 0:1], None, ALU.is_le)
            link(last)
            link(dve.tensor_reduce(key[:, :], ge[:, :, :], axis=AX, op=ALU.add))
            link(dve.tensor_tensor(key[:, :], key[:, :], tcol[:, :], ALU.add))
            link(dve.tensor_scalar(live[:, :], tcol[:, :], 0.0, None, ALU.is_gt))
            link(dve.tensor_tensor(key[:, :], key[:, :], live[:, :], ALU.mult))
            for c in range(CH):
                last = dve.tensor_scalar(hit[:, c, :], iota_f[:, :], key[:, c:c + 1], None, ALU.is_ge)
            last.then_inc(hits_ready, 1)
            for g in range(3):
                evac("n0", g, None, HID, None, 0)
            dve.wait_ge(counts_ready, 1)
            link(dve.tensor_scalar(step_edge, ps[:, 0, 0:STEPS], -1.0, None, ALU.add))
            for c in range(CH):
                last = dve.tensor_scalar(hit[:, c, :], step_edge, tcol[:, c:c + 1], None, ALU.is_equal)
            last.then_inc(picks_ready, 1)
            link(dve.tensor_tensor(step_base, iota_f[:, :], step_edge, ALU.subtract))
            dve.tensor_copy(step_tile[:, 0:STEPS], step_base)
            link(dve.tensor_copy(step_tile[:, STEPS:STEPS + HALF], step_base[:, 0:HALF]))
            link(dve.tensor_scalar(step_base, step_base, float(NT), None, ALU.mult))
            for g in range(3, 5):
                evac("n0", g, None, HID, None, 0)
            dve.wait_ge(rows_picked, 2)
            dve.tensor_copy(step_src[:, :], ps[:, 1, 0:STEPS])
            link(dve.tensor_tensor(step_dst[:, 0:STEPS], ps[:, 0, 0:STEPS], step_base, ALU.subtract))
            dve.memset(slots[:, :, HID:WMAX], 1.0)
            link(dve.tensor_copy(step_dst[:, STEPS:STEPS + HALF], step_dst[:, 0:HALF]))
            dve.sem_inc(table_ready, 1)
            for g in range(5, NG):
                evac("n0", g, None, HID, None, 0)
            dve.wait_ge(bias_loaded, 16 * (3 + 11 * LAYERS))
            for g, (t0, t1) in enumerate(GR):
                evac("s0", g, S[:, t0:t1, :], HID, row_of(bias_s[:, 0, :], g, HID))
            build_onehots(0, 0).then_inc(onehot_ready, 1)
            sage_steps(0, HID + 1)
            deg = acc[0:NT, :, HID]
            dve.tensor_scalar(deg_pos[:, :], deg, 0.0, None, ALU.is_gt)
            link(dve.tensor_scalar(inv_deg[:, :], deg, 1.0, None, ALU.max))
            link(dve.reciprocal(inv_deg[:, :], inv_deg[:, :]))
            link(dve.tensor_tensor(inv_deg[:, :], inv_deg[:, :], deg_pos[:, :], ALU.mult))
            for s, w, bias in ((1, HID, bias_s[:, 1, :]), (2, D, bias_n[:, :])):
                for g in range(NG):
                    combine(g, HID).then_inc(comb_ready, 1)
                for g in range(NG):
                    evac(f"n{s}", g, None, w, None, s)
                for g, (t0, t1) in enumerate(GR):
                    evac(f"s{s}", g, S[:, t0:t1, 0:w], w, row_of(bias, g, w))
                dve.wait_ge(m_evac, 3 + M_UNIT[(f"s{s}", NG - 1)] + 1)
                sage_steps(s, w)

            def node_out(name, g):
                t0, t1 = GR[g]
                n = M_UNIT[(name, g)]
                stage, l = (name, 0) if name == "emb" else (name[:-1], int(name[-1]))
                if stage == "emb":
                    evac(name, g, h[:, t0:t1, :], D)
                    dve.wait_ge(m_evac, 3 + n + 1)
                    dve.sem_inc(h_ready, 1)
                elif stage == "kv":
                    evac(name, g, None, 2 * D,
                         row_of(brow[:, l, 0:2, :].rearrange("p a n -> p (a n)"), g, 2 * D), SAGE + l)
                elif stage == "q":
                    evac(name, g, q[:, t0:t1, :], D, row_of(brow[:, l, 2, :], g, D))
                elif stage == "o":
                    dve.wait_ge(h_biased, l + 1)
                    evac(name, g, hx[:, t0:t1, :], D, h[:, t0:t1, :])
                    dve.wait_ge(m_evac, 3 + n + 1)
                    norm_stats(g, lambda t: hx[:, t, :])
                elif stage == "f":
                    dve.wait_ge(hx_biased, l * NG + g + 1)
                    evac(name, g, h[:, t0:t1, :], D, y[:, t0:t1, :])
                    dve.wait_ge(m_evac, 3 + n + 1)
                    norm_stats(g, lambda t: h[:, t, :])

            def hx_out(l, g):
                norm_apply(f"hx{l}", g, lambda t: hx[:, t, :], lambda t: hx[:, t, :], l, 5, 6).then_inc(hx_ready, 1)

            def h_out(l, g):
                t0, t1 = GR[g]
                last = norm_apply(f"h{l}", g, lambda t: h[:, t, :], lambda t: h[:, t, :], l, 7, 8)
                if l + 1 < LAYERS:
                    last.then_inc(h_ready, 1)
                else:
                    link(last)
                    dve.tensor_tensor(y[:, t0:t1, :], xs[:, t0:t1, :], h[:, t0:t1, :], ALU.add)\
                       .then_inc(out_ready, 1)

            for w in range(NG + 2):
                if w < NG:
                    t0, t1 = GR[w]
                    link(combine(w, D))
                    link(dve.scalar_tensor_tensor(xs[:, t0:t1, :], acc[0:NT, t0:t1, 0:D], 0.0, xs[:, t0:t1, :],
                                                  ALU.max, ALU.add))
                    norm_stats(w, lambda t: xs[:, t, :])
                if 0 < w <= NG:
                    node_out("emb", w - 1)
                if w < NG:
                    norm_apply("x2", w, lambda t: xs[:, t, :], lambda t: y[:, t, :]).then_inc(y_ready, 1)
                if w == NG:
                    dve.sem_inc(x_summed, 1)
                if w > 1:
                    node_out("kv0", w - 2)
            for g in range(NG):
                node_out("q0", g)
            dve.sem_inc(prod_done, 1)

            for l in range(LAYERS):
                first = (SAGE + l) * STEPS
                dve.wait_ge(m_evac, 3 + M_UNIT[(f"q{l}", NG - 1)] + 1)
                dve.wait_ge(acc_zeroed, SAGE + l + 1)

                def attention_half(m, it_plus, half, first_step, add_before):
                    lo = half * HALF
                    dve.wait_ge(q_done, m + l + 1)
                    for j in range(HALF):
                        dve.wait_ge(gathered[lo + j], ((SAGE + l) * ITERS + it_plus) * 16)
                    dve.scalar_tensor_tensor(prod[:, :, :], slots[:, lo:lo + HALF, 0:D], DH ** -0.5, psQ,
                                             ALU.mult, ALU.mult).then_inc(prod_done, 1)
                    dve.wait_ge(prod_done, m + 2)
                    dve.tensor_reduce(score[:, :, :],
                                      prod[:, :, :].rearrange("p j (h e) -> p j h e", h=HEADS),
                                      axis=AX, op=ALU.add).then_inc(score_done, 1)
                    dve.wait_ge(score_done, m + 1)
                    dve.tensor_scalar(clipped[:, :, :], score[:, :, :], -5.0, 5.0, ALU.max, ALU.min)\
                       .then_inc(clip_done, 1)
                    dve.wait_ge(onehot_free, SAGE * HALVES + m + 2)
                    build_onehots(1 - half, first_step + HALF).then_inc(onehot_ready, 1)
                    if add_before:
                        add_half(first_step - HALF, psA, MW, SAGE * STEPS + (m - 1) * HALF, 2)
                    dve.wait_ge(exp_done, m + 1)
                    dve.tensor_tensor(
                        msg[:, half, :, 0:D].rearrange("p j (h e) -> p j h e", h=HEADS),
                        slots[:, lo:lo + HALF, D:2 * D].rearrange("p j (h e) -> p j h e", h=HEADS),
                        bc(msg[:, half, :, D:MW].unsqueeze(3), [P, HALF, HEADS, DH]), ALU.mult)\
                       .then_inc(msg_ready, 1)
                    dve.wait_ge(msg_ready, m + 1)
                    dve.sem_inc(half_free, 1)

                m0 = l * HALVES
                attention_half(m0, 1, 0, 0, False)
                with dve.Fori(0, ITERS - 1) as it:
                    attention_half(m0 + it * 2 + 1, it + 1, 1, it * RING + HALF, True)
                    attention_half(m0 + it * 2 + 2, it + 2, 0, it * RING + RING, True)
                attention_half(m0 + HALVES - 1, ITERS, 1, STEPS - HALF, True)
                add_half(STEPS - HALF, psA, MW, first + STEPS - HALF, 2)
                dve.wait_ge(added, 2 + first + STEPS)

                def normalise(g):
                    t0, t1 = GR[g]
                    link(dve.tensor_scalar(zr[:, t0:t1, :], acc[0:NT, t0:t1, D:MW], Z_EPS, None, ALU.add))
                    link(dve.reciprocal(zr[:, t0:t1, :], zr[:, t0:t1, :]))
                    dve.tensor_tensor(
                        y[:, t0:t1, :].rearrange("p t (h e) -> p t h e", h=HEADS),
                        acc[0:NT, t0:t1, 0:D].rearrange("p t (h e) -> p t h e", h=HEADS),
                        bc(zr[:, t0:t1, :].unsqueeze(3), [NT, t1 - t0, HEADS, DH]), ALU.mult).then_inc(y_ready, 1)

                for w in range(NG + 3):
                    if w < NG:
                        normalise(w)
                    if 0 <= w - 1 < NG:
                        node_out(f"o{l}", w - 1)
                    if 0 <= w - 2 < NG:
                        node_out(f"f{l}", w - 2)
                    if 0 <= w - 1 < NG:
                        hx_out(l, w - 1)
                    if 0 <= w - 2 < NG:
                        h_out(l, w - 2)
                    if l + 1 < LAYERS and 0 <= w - 3 < NG:
                        node_out(f"kv{l + 1}", w - 3)
                if l + 1 < LAYERS:
                    for g in range(NG):
                        node_out(f"q{l + 1}", g)


_INS = ['x', 'src', 'dst', 'L0_gnn_Ws0', 'L0_gnn_Wn0', 'L0_gnn_b0', 'L0_gnn_Ws1', 'L0_gnn_Wn1', 'L0_gnn_b1',
        'L0_gnn_Ws2', 'L0_gnn_Wn2', 'L0_gnn_b2', 'L1_gnn_W_emb', 'L1_gnn_Wq', 'L1_gnn_bq', 'L1_gnn_Wk', 'L1_gnn_bk',
        'L1_gnn_Wv', 'L1_gnn_bv', 'L1_gnn_Wo', 'L1_gnn_bo', 'L1_gnn_ln1_w', 'L1_gnn_ln1_b', 'L1_gnn_Wf1',
        'L1_gnn_bf1', 'L1_gnn_Wf2', 'L1_gnn_bf2', 'L1_gnn_ln2_w', 'L1_gnn_ln2_b']
_OUTS = [((3125, 128), 'float32')]


def kernel(**inputs):
    import numpy as _np
    import concourse.bacc as _bacc
    from concourse import mybir as _mybir
    from concourse.bass_utils import run_bass_kernel_spmd as _run

    nc = _bacc.Bacc("TRN2", target_bir_lowering=False, num_devices=1)
    arrays, args = {}, []
    for name in _INS:
        a = _np.ascontiguousarray(inputs[name])
        arrays[f"in_{name}_dram"] = a
        args.append(nc.dram_tensor(f"in_{name}_dram", a.shape, _mybir.dt.from_np(a.dtype), kind="ExternalInput").ap())
    for i, (shape, dtype) in enumerate(_OUTS):
        dt = _mybir.dt.from_np(_np.dtype(dtype))
        args.append(nc.dram_tensor(f"out_{i}_dram", shape, dt, kind="ExternalOutput").ap())
    gnn_kernel(nc, *args)
    r = _run(nc, [arrays], core_ids=[0])
    return r.results[0]["out_0_dram"]
```
